# Optimizing a Trainium2 kernel written in Bass

```python
import numpy as np
import jax
import jax.numpy as jnp

def _softmax(x, axis=-1):
    return jax.nn.softmax(x, axis=axis)
def _gelu(x):
    return jax.nn.gelu(x, approximate=True)
def _silu(x):
    return jax.nn.silu(x)
def _sigmoid(x):
    return jax.nn.sigmoid(x)
def _layernorm(x, axis=-1, eps=1e-5):
    m = jnp.mean(x, axis=axis, keepdims=True)
    v = jnp.var(x, axis=axis, keepdims=True)
    return (x - m) / jnp.sqrt(v + eps)
def _scatter_add(tgt, idx, src, axis=0):
    return tgt.at[idx].add(src)
def _segment_sum(src, seg, n):
    return jax.ops.segment_sum(src, seg, n)

kernel_name = 'mk_conv_preact_d1_conv_nchw128_236278'

def setup_inputs(seed: int = 0):
    np.random.seed(seed)
    _w = jnp.asarray
    def _rec_inputs():
        import jax
        import jax.numpy as jnp
        _gk = jax.random.key(seed)
        x = -0.000125 + 0.9999 * jax.random.normal(jax.random.fold_in(_gk, 1), (16, 128, 256, 64), jnp.float32)
        return x
    x = _rec_inputs()
    def _L0_conv_setup():
        import jax, jax.numpy as jnp
        import numpy as np

        def _conv1x1_relu(x, w, b):
            y = jnp.einsum('oc,bchw->bohw', w, x) + b[None, :, None, None]
            return jax.nn.relu(y)
        key = jax.random.key(seed)
        ks = jax.random.split(key, 9)
        B, C, H, W = (16, 128, 256, 64)
        s = 1.0 / np.sqrt(C)
        return {'rep': jax.random.normal(ks[0], (B, C, H, W), jnp.float32), 'wq': jax.random.normal(ks[1], (C, C), jnp.float32) * s, 'bq': jax.random.normal(ks[2], (C,), jnp.float32) * 0.02, 'wk': jax.random.normal(ks[3], (C, C), jnp.float32) * s, 'bk': jax.random.normal(ks[4], (C,), jnp.float32) * 0.02, 'wv': jax.random.normal(ks[5], (C, C), jnp.float32) * s, 'bv': jax.random.normal(ks[6], (C,), jnp.float32) * 0.02, 'wfc': jax.random.normal(ks[7], (C, C), jnp.float32) * s, 'bfc': jax.random.normal(ks[8], (C,), jnp.float32) * 0.02}
    _L0_conv_all = _L0_conv_setup()
    _L0_conv_in = {k: v for k, v in _L0_conv_all.items() if k in ('wq', 'bq', 'wk', 'bk', 'wv', 'bv', 'wfc', 'bfc', )}
    del _L0_conv_all

    return {
        "x": x,
        "L0_conv_wq": _L0_conv_in["wq"],
        "L0_conv_bq": _L0_conv_in["bq"],
        "L0_conv_wk": _L0_conv_in["wk"],
        "L0_conv_bk": _L0_conv_in["bk"],
        "L0_conv_wv": _L0_conv_in["wv"],
        "L0_conv_bv": _L0_conv_in["bv"],
        "L0_conv_wfc": _L0_conv_in["wfc"],
        "L0_conv_bfc": _L0_conv_in["bfc"],
    }

def reference(x, L0_conv_wq, L0_conv_bq, L0_conv_wk, L0_conv_bk, L0_conv_wv, L0_conv_bv, L0_conv_wfc, L0_conv_bfc):
    import jax
    import jax.numpy as jnp
    def _L0_conv_ref(rep, wq, bq, wk, bk, wv, bv, wfc, bfc):
        import jax, jax.numpy as jnp
        import numpy as np

        def _conv1x1_relu(x, w, b):
            y = jnp.einsum('oc,bchw->bohw', w, x) + b[None, :, None, None]
            return jax.nn.relu(y)
        C = rep.shape[1]
        q = _conv1x1_relu(rep, wq, bq).transpose(0, 3, 2, 1)
        k = _conv1x1_relu(rep, wk, bk).transpose(0, 3, 2, 1)
        v = _conv1x1_relu(rep, wv, bv).transpose(0, 3, 2, 1)
        attn = jnp.einsum('bwhc,bwgc->bwhg', q, k) / jnp.sqrt(jnp.asarray(C, q.dtype))
        attn = jax.nn.softmax(attn, axis=-1)
        out = jnp.einsum('bwhg,bwgc->bwhc', attn, v)
        out = out.transpose(0, 3, 2, 1)
        return _conv1x1_relu(out, wfc, bfc)

    def _gn(v, G=32, eps=1e-5):
        B_, C_, H_, W_ = v.shape
        g = v.reshape(B_, G, C_ // G, H_, W_)
        m = jnp.mean(g, axis=(2, 3, 4), keepdims=True)
        s = jnp.var(g, axis=(2, 3, 4), keepdims=True)
        return ((g - m) / jnp.sqrt(s + eps)).reshape(v.shape)

    def _ln_c(v, eps=1e-6):
        m = jnp.mean(v, axis=1, keepdims=True)
        s = jnp.var(v, axis=1, keepdims=True)
        return (v - m) / jnp.sqrt(s + eps)

    def _ln_t(v, eps=1e-5):
        m = jnp.mean(v, axis=-1, keepdims=True)
        s = jnp.var(v, axis=-1, keepdims=True)
        return (v - m) / jnp.sqrt(s + eps)

    def _to_tokens(v):
        B_, C_, H_, W_ = v.shape
        return v.reshape(B_, C_, H_ * W_).transpose(0, 2, 1)
    def _from_tokens(t, like):
        B_, C_, H_, W_ = like.shape
        return t.transpose(0, 2, 1).reshape(B_, C_, H_, W_)

    x = x + _L0_conv_ref(_gn(x), L0_conv_wq, L0_conv_bq, L0_conv_wk, L0_conv_bk, L0_conv_wv, L0_conv_bv, L0_conv_wfc, L0_conv_bfc)
    return x


_drawn_inputs = setup_inputs


def setup_inputs(seed=0):
    import zlib

    import numpy as np

    out = dict(_drawn_inputs(seed))
    spreads = {}
    factors = {'L0_conv_wq': 3.861,
     'L0_conv_bq': 8.0,
     'L0_conv_wk': 3.132,
     'L0_conv_bk': 8.0,
     'L0_conv_bv': 7.481,
     'L0_conv_bfc': 3.952}
    for name, (base, spread) in spreads.items():
        noise = np.random.default_rng([zlib.crc32(name.encode()), seed]).standard_normal(out[name].shape)
        drawn = base * np.exp(spread * noise) if base else spread * noise
        out[name] = jnp.asarray(drawn.astype(out[name].dtype))
    for name, factor in factors.items():
        out[name] = (out[name] * factor).astype(out[name].dtype)
    return out
```

```python
from contextlib import ExitStack

import concourse.bass as bass
from concourse import mybir

F32 = mybir.dt.float32
F16 = mybir.dt.float16
ALU = mybir.AluOpType
ACT = mybir.ActivationFunctionType
AX = mybir.AxisListType

PAIR = 2
CHUNKS = 8
LEAD = 3
GROUPS = 32
EPS = 1e-5


def build(nc, x, wq, bq, wk, bk, wv, bv, wfc, bfc, out):
    B, C, H, W = x.shape
    PAIRS = W // PAIR
    N = B * PAIRS
    HW = H * W
    COLS = PAIR * H
    HALVES = H // 128
    GC = C // GROUPS
    CHUNK = HW // CHUNKS
    PIECE = 512
    PIECES = HW // PIECE
    PER_CHUNK = CHUNK // PIECE
    SCALE = float(C) ** -0.5
    assert C == 128 and H == 256 and COLS == 512 and B % 2 == 0 and PAIRS == 32

    x_dram = x.rearrange("b c h w -> b c (h w)")
    out_dram = out.rearrange("b c h w -> b c (h w)")

    with ExitStack() as ctx:
        def sb(name, shape, dt=F32):
            return ctx.enter_context(nc.sbuf_tensor(name, shape, dt))

        def bank(name):
            return ctx.enter_context(nc.psum_tensor(name, [128, 512], F32))

        def sem(name):
            return ctx.enter_context(nc.semaphore(name))

        X = [sb(f"x_sample{n}", [C, HW]) for n in range(2)]
        Xhw = [t[:, :].rearrange("c (h w) -> c h w", w=W) for t in X]
        xn = [sb(f"xn{n}", [C, COLS]) for n in range(2)]
        x_hi = [sb(f"x_hi{n}", [C, COLS], F16) for n in range(2)]
        x_lo = [sb(f"x_lo{n}", [C, COLS], F16) for n in range(2)]
        q32, k32 = sb("q32", [C, COLS]), sb("k32", [C, COLS])
        q_hi, q_lo = sb("q_hi", [C, COLS], F16), sb("q_lo", [C, COLS], F16)
        k_hi, k_lo = sb("k_hi", [C, COLS], F16), sb("k_lo", [C, COLS], F16)
        v_sb = [sb(f"v{n}", [128, PAIR, HALVES, C]) for n in range(2)]
        probs = [[sb(f"probs{n}_w{w}", [128, HALVES, H]) for w in range(PAIR)] for n in range(2)]
        probsT = [sb(f"probsT_w{w}", [128, HALVES, H]) for w in range(PAIR)]
        negmax = [sb(f"negmax_w{w}", [128, HALVES]) for w in range(PAIR)]
        sums = [sb(f"sums_w{w}", [128, HALVES]) for w in range(PAIR)]
        rsum = [sb(f"rsum_w{w}", [128, HALVES]) for w in range(PAIR)]
        o_hi, o_lo = sb("o_hi", [C, COLS], F16), sb("o_lo", [C, COLS], F16)
        y = [sb(f"y{n}", [C, COLS]) for n in range(2)]

        ident = sb("ident", [128, 128])
        w_raw = sb("w_raw", [128, 4, C])
        wT_hi, wT_lo = sb("wT_hi", [C, 4, C], F16), sb("wT_lo", [C, 4, C], F16)
        b_raw = sb("b_raw", [C, 4])
        bq_scaled = sb("bq_scaled", [C, 1])
        bv_row = sb("bv_row", [1, C])
        minus_one = sb("minus_one", [1, 128])
        neg_bv = sb("neg_bv", [128, PAIR * HALVES, C])

        pieces = sb("pieces", [C, PIECES, 6])
        stat = sb("stat", [C, 32])
        statT, spreadT = sb("statT", [C, 32]), sb("spreadT", [C, 32])
        groupT = sb("groupT", [C, 32 // GC])
        group = sb("group", [C, 32])
        group_sq = sb("group_sq", [C, 32])
        var_eps = sb("var_eps", [C, 1])
        minus_half = sb("minus_half", [C, 1])
        mean_g = sb("mean_g", [C, 1])
        rstd_g = sb("rstd_g", [C, 1])

        q_ps, k_ps, vf_ps, o_ps = bank("q_ps"), bank("k_ps"), bank("vf_ps"), bank("o_ps")
        s_ps = [bank(f"s_ps{w}") for w in range(PAIR)]
        t_ps = [bank(f"t_ps{w}") for w in range(PAIR)]

        params_in = sem("params_in")
        loaded = [[sem(f"loaded{n}_{c}") for c in range(CHUNKS)] for n in range(2)]
        stored = [sem(f"stored{c}") for c in range(CHUNKS)]
        ident_done, wT_in_psum, wT_split, setup_vec = sem("ident_done"), sem("wT_in_psum"), sem("wT_split"), sem("setup_vec")
        xn_done, x_hi_done, x_lo_done = sem("xn_done"), sem("x_hi_done"), sem("x_lo_done")
        q_in_psum, k_in_psum, v_in_psum = sem("q_in_psum"), sem("k_in_psum"), sem("v_in_psum")
        q32_done, k32_done, v_done = sem("q32_done"), sem("k32_done"), sem("v_done")
        q_hi_done, q_lo_done, k_hi_done, k_lo_done = sem("q_hi_done"), sem("q_lo_done"), sem("k_hi_done"), sem("k_lo_done")
        s_in_psum = [sem(f"s_in_psum_w{w}") for w in range(PAIR)]
        max_done = [sem(f"max_done_w{w}") for w in range(PAIR)]
        exp_done = [sem(f"exp_done_w{w}") for w in range(PAIR)]
        rsum_done = [sem(f"rsum_done_w{w}") for w in range(PAIR)]
        probs_done = [sem(f"probs_done_w{w}") for w in range(PAIR)]
        t_in_psum = [sem(f"t_in_psum_w{w}") for w in range(PAIR)]
        probsT_done = [sem(f"probsT_done_w{w}") for w in range(PAIR)]
        o_in_psum, o_hi_done, o_lo_done = sem("o_in_psum"), sem("o_hi_done"), sem("o_lo_done")
        f_in_psum, y_done, res_done = sem("f_in_psum"), sem("y_done"), sem("res_done")
        pieces_done = sem("pieces_done")
        stat_chain, var_done, rstd_done = sem("stat_chain"), sem("var_done"), sem("rstd_done")

        def live(j):
            return not isinstance(j, int) or 0 <= j < N

        def wait(eng, semaphore, value):
            if not isinstance(value, int) or value > 0:
                eng.wait_ge(semaphore, value)

        def steps(eng, step, first, last):
            lo, hi = max(first, LEAD), min(last, N - LEAD - 1)
            hi -= (hi - lo + 1) % 2
            for i in range(first, lo):
                step(i, i % 2)
            with_loop = hi >= lo
            if with_loop:
                with eng.Fori(lo, hi, 2) as i:
                    step(i, lo % 2)
                    step(i + 1, (lo + 1) % 2)
            for i in range(hi + 1 if with_loop else lo, last + 1):
                step(i, i % 2)

        block = ctx.enter_context(nc.Block())

        @block.sync
        def _(sp):
            for c in range(CHUNKS):
                sp.dma_start(X[0][:, c * CHUNK:(c + 1) * CHUNK],
                             x_dram[0, :, c * CHUNK:(c + 1) * CHUNK]).then_inc(loaded[0][c], 16)
                if c == 0:
                    for n, w_dram in enumerate((wq, wk, wv, wfc)):
                        sp.dma_start(w_raw[:, n, :], w_dram).then_inc(params_in, 16)
                    for n, b_dram in enumerate((bq, bk, bv, bfc)):
                        sp.dma_start(b_raw[:, n:n + 1], b_dram.rearrange("(c a) -> c a", a=1)).then_inc(params_in, 16)
                    sp.dma_start(bv_row[:, :], bv.rearrange("(a c) -> a c", a=1)).then_inc(params_in, 16)
            for c in range(CHUNKS):
                sp.dma_start(X[1][:, c * CHUNK:(c + 1) * CHUNK],
                             x_dram[1, :, c * CHUNK:(c + 1) * CHUNK]).then_inc(loaded[1][c], 16)

            def store(s, buf, c):
                sp.dma_start(out_dram[s, :, c * CHUNK:(c + 1) * CHUNK],
                             X[buf][:, c * CHUNK:(c + 1) * CHUNK]).then_inc(stored[c], 16)

            def load(s, buf, c):
                sp.wait_ge(stored[c], (s - 1) * 16)
                sp.dma_start(X[buf][:, c * CHUNK:(c + 1) * CHUNK],
                             x_dram[s, :, c * CHUNK:(c + 1) * CHUNK]).then_inc(loaded[buf][c], 16)

            with sp.Fori(0, B - 3, 2) as s0:
                for buf in range(2):
                    s = s0 + buf
                    sp.wait_ge(res_done, (s + 1) * PAIRS)
                    for c in range(CHUNKS + 1):
                        if c < CHUNKS:
                            store(s, buf, c)
                        if c > 0:
                            load(s + 2, buf, c - 1)
            for s in (B - 2, B - 1):
                sp.wait_ge(res_done, (s + 1) * PAIRS)
                for c in range(CHUNKS):
                    store(s, s % 2, c)
            for c in range(CHUNKS):
                sp.wait_ge(stored[c], B * 16)

        @block.tensor
        def _(pe):
            def product(psum, pairs):
                for n, (stationary, moving) in enumerate(pairs):
                    last = nc.tensor.matmul(psum, stationary, moving, start=(n == 0), stop=(n == len(pairs) - 1))
                return last

            def step(i, par):
                nxt = 1 - par
                if live(i):
                    if isinstance(i, int) and i < 2:
                        wait(pe, v_done, i)
                    wait(pe, y_done, i - 2)
                    for t in range(PAIR * HALVES):
                        tok = slice(t * 128, (t + 1) * 128)
                        last = product(vf_ps[:, t * C:(t + 1) * C],
                                       [(x_hi[par][:, tok], wT_hi[:, 2, :]), (x_hi[par][:, tok], wT_lo[:, 2, :]),
                                        (x_lo[par][:, tok], wT_hi[:, 2, :])])
                    last.then_inc(v_in_psum, 1)
                    wait(pe, k_lo_done, i + 1)
                    wait(pe, q_lo_done, i + 1)
                    for w in range(PAIR):
                        wait(pe, exp_done[w], i)
                        for a in range(HALVES):
                            rows = slice(w * H + a * 128, w * H + (a + 1) * 128)
                            keys = slice(w * H, (w + 1) * H)
                            last = product(s_ps[w][:, a * H:(a + 1) * H],
                                           [(q_hi[:, rows], k_hi[:, keys]), (q_hi[:, rows], k_lo[:, keys]),
                                            (q_lo[:, rows], k_hi[:, keys])])
                        last.then_inc(s_in_psum[w], 1)
                if live(i + 1):
                    wait(pe, x_lo_done, i + 2)
                    for m, psum, ready in ((0, q_ps, q_in_psum), (1, k_ps, k_in_psum)):
                        product(psum[:, :], [(wT_hi[:, m, :], x_hi[nxt][:, :]), (wT_lo[:, m, :], x_hi[nxt][:, :]),
                                             (wT_hi[:, m, :], x_lo[nxt][:, :])]).then_inc(ready, 1)
                if live(i - 1):
                    for w in range(PAIR):
                        wait(pe, probs_done[w], i)
                        for a in range(HALVES):
                            for b in range(HALVES):
                                last = nc.tensor.transpose(t_ps[w][:, b * H + a * 128:b * H + (a + 1) * 128],
                                                           probs[nxt][w][:, a, b * 128:(b + 1) * 128], ident[:, :])
                        last.then_inc(t_in_psum[w], 1)
                if live(i - 2):
                    wait(pe, o_lo_done, i - 1)
                    wait(pe, v_done, min(i + 1, N) if isinstance(i, int) else i + 1)
                    product(vf_ps[:, :], [(wT_hi[:, 3, :], o_hi[:, :]), (wT_lo[:, 3, :], o_hi[:, :]),
                                          (wT_hi[:, 3, :], o_lo[:, :])]).then_inc(f_in_psum, 1)
                if live(i - 1):
                    if not live(i - 2) or not live(i):
                        wait(pe, v_done, i)
                    for w in range(PAIR):
                        wait(pe, probsT_done[w], i)
                        last = product(o_ps[:, w * H:(w + 1) * H],
                                       [(v_sb[nxt][:, w, b, :], probsT[w][:, b, :]) for b in range(HALVES)])
                    last.then_inc(o_in_psum, 1)

            pe.wait_ge(ident_done, 2)
            pe.wait_ge(params_in, 9 * 16)
            for n in range(4):
                last = nc.tensor.transpose(q_ps[:, n * C:(n + 1) * C], w_raw[:, n, :], ident[:, :])
            last.then_inc(wT_in_psum, 1)
            pe.wait_ge(setup_vec, 1)
            nc.tensor.matmul(k_ps[:, 0:C], minus_one[:, :], bv_row[:, :], start=True, stop=True).then_inc(wT_in_psum, 1)
            pe.wait_ge(wT_split, 4)
            steps(pe, step, -1, N + 1)

        @block.scalar
        def _(act):
            def softmax_exp(j, par, w):
                wait(act, max_done[w], j + 1)
                for a in range(HALVES):
                    last = nc.scalar.activation(probs[par][w][:, a, :], s_ps[w][:, a * H:(a + 1) * H], ACT.Exp,
                                                bias=negmax[w][:, a:a + 1], accum_out=sums[w][:, a:a + 1])
                last.then_inc(exp_done[w], 1)

            def step(i, par):
                nxt = 1 - par
                if live(i - 1):
                    softmax_exp(i - 1, nxt, 1)
                if live(i + 2):
                    wait(act, xn_done, i + 3)
                    wait(act, v_in_psum, i + 1)
                    nc.scalar.activation(x_hi[par][:, :], xn[par][:, :], ACT.Copy).then_inc(x_hi_done, 1)
                if live(i - 2):
                    wait(act, v_in_psum if live(i) else o_in_psum, i + 1 if live(i) else i - 1)
                    nc.scalar.activation(o_hi[:, :], o_ps[:, :], ACT.Identity,
                                         bias=b_raw[:, 2:3]).then_inc(o_hi_done, 1)
                if live(i + 1):
                    wait(act, q_in_psum, i + 2)
                    nc.scalar.activation(q32[:, :], q_ps[:, :], ACT.Relu, bias=bq_scaled[:, :],
                                         scale=SCALE).then_inc(q32_done, 1)
                    wait(act, k_in_psum, i + 2)
                    nc.scalar.activation(k32[:, :], k_ps[:, :], ACT.Relu, bias=b_raw[:, 1:2]).then_inc(k32_done, 1)
                if live(i - 1):
                    wait(act, t_in_psum[0], i)
                    nc.scalar.activation(probsT[0][:, :, :], t_ps[0][:, :].rearrange("p (b h) -> p b h", h=H),
                                         ACT.Copy).then_inc(probsT_done[0], 1)
                if live(i + 1):
                    wait(act, q32_done, i + 2)
                    nc.scalar.activation(q_hi[:, :], q32[:, :], ACT.Copy).then_inc(q_hi_done, 1)
                if live(i - 2):
                    wait(act, f_in_psum, i - 1)
                    wait(act, res_done, i - 3)
                    nc.scalar.activation(y[par][:, :], vf_ps[:, :], ACT.Relu, bias=b_raw[:, 3:4]).then_inc(y_done, 1)
                if live(i):
                    softmax_exp(i, par, 0)

            act.wait_ge(params_in, 9 * 16)
            act.wait_ge(setup_vec, 2)
            steps(act, step, -2, N + 1)

        @block.gpsimd
        def _(pool):
            def rstd(s):
                pool.wait_ge(var_done, s + 1)
                nc.gpsimd.tensor_tensor(rstd_g[:, :], var_eps[:, :], minus_half[:, :], ALU.pow).then_inc(rstd_done, 1)

            def step(i, par):
                nxt = 1 - par
                if live(i - 1):
                    wait(pool, rsum_done[1], i)
                    nc.gpsimd.tensor_tensor(
                        probs[nxt][1][:, :, :], probs[nxt][1][:, :, :],
                        rsum[1][:, :].rearrange("p (a o) -> p a o", o=1).to_broadcast([128, HALVES, H]),
                        ALU.mult).then_inc(probs_done[1], 1)
                if live(i + 2):
                    wait(pool, x_hi_done, i + 3)
                    nc.gpsimd.tensor_tensor(x_lo[par][:, :], xn[par][:, :], x_hi[par][:, :],
                                            ALU.subtract).then_inc(x_lo_done, 1)
                if live(i + 1):
                    wait(pool, k_hi_done, i + 2)
                    nc.gpsimd.tensor_tensor(k_lo[:, :], k32[:, :], k_hi[:, :], ALU.subtract).then_inc(k_lo_done, 1)
                    wait(pool, q_hi_done, i + 2)
                    nc.gpsimd.tensor_tensor(q_lo[:, :], q32[:, :], q_hi[:, :], ALU.subtract).then_inc(q_lo_done, 1)

            nc.gpsimd.memset(ident[:, :], 0.0).then_inc(ident_done, 1)
            pool.wait_ge(ident_done, 1)
            nc.gpsimd.affine_select(out=ident[:, :], in_=ident[:, :], compare_op=ALU.not_equal, fill=1.0, base=0,
                                    pattern=[[-1, 128]], channel_multiplier=1).then_inc(ident_done, 1)
            pool.wait_ge(setup_vec, 1)
            rstd(0)
            steps(pool, step, -2, PAIRS - LEAD - 1)
            with pool.Fori(1, B) as s:
                rstd(s)
                with pool.Fori(0, PAIRS - 1, 2) as p:
                    step(s * PAIRS + p - LEAD, 1)
                    step(s * PAIRS + p - LEAD + 1, 0)
            for i in range(N - LEAD, N + 1):
                step(i, i % 2)

        @block.vector
        def _(dve):
            def measure(buf, n):
                return nc.vector.bn_stats(pieces[:, n, :], X[buf][:, bass.ds(n * PIECE, PIECE)])

            def chained(s, n, instruction):
                instruction.then_inc(stat_chain, 1)
                dve.wait_ge(stat_chain, s * CHAIN + n)

            CHAIN = 12

            def spread(s, n, source, result):
                chained(s, n, nc.vector.transpose(statT[:, :], source))
                chained(s, n + 1, nc.vector.tensor_reduce(groupT[:, :], statT[:, :].rearrange("p (g c) -> p g c", c=GC),
                                                          AX.X, ALU.add))
                chained(s, n + 2, nc.vector.tensor_scalar(
                    spreadT[:, :].rearrange("p (g c) -> p g c", c=GC),
                    groupT[:, :].rearrange("p (g a) -> p g a", a=1).to_broadcast([C, 32 // GC, GC]),
                    1.0 / GC, None, ALU.mult))
                chained(s, n + 3, nc.vector.transpose(result, spreadT[:, :]))

            def aggregate(s):
                dve.wait_ge(pieces_done, s + 1)
                nc.vector.memset(stat[:, 2:32], 0.0)
                chained(s, 1, nc.vector.bn_aggr(stat[:, 0:2], pieces[:, :, :].rearrange("p n k -> p (n k)")))

            def group_means(s):
                spread(s, 2, stat[:, :], group[:, :])

            def squared_distances(s):
                chained(s, 6, nc.vector.tensor_tensor(stat[:, 2:3], stat[:, 0:1], group[:, 0:1], ALU.subtract))
                chained(s, 7, nc.vector.tensor_tensor(stat[:, 3:4], stat[:, 2:3], stat[:, 2:3], ALU.mult))
                spread(s, 8, stat[:, :], group_sq[:, :])

            def hand_over(s):
                wait(dve, xn_done, s * PAIRS)
                chained(s, 12, nc.vector.tensor_copy(mean_g[:, :], group[:, 0:1]))
                nc.vector.tensor_scalar(var_eps[:, :], group[:, 1:2], group_sq[:, 3:4], EPS,
                                        ALU.add, ALU.add).then_inc(var_done, 1)

            statistics = (aggregate, group_means, squared_distances, hand_over)

            def step(i, par, buf, p, measured=None):
                nxt = 1 - par
                static = isinstance(p, int)
                if live(i - 1):
                    wait(dve, exp_done[0], i)
                    nc.vector.reciprocal(rsum[0][:, :], sums[0][:, :]).then_inc(rsum_done[0], 1)
                    wait(dve, rsum_done[0], i)
                    for a in range(HALVES):
                        last = nc.vector.tensor_scalar(probs[nxt][0][:, a, :], probs[nxt][0][:, a, :],
                                                       rsum[0][:, a:a + 1], None, ALU.mult)
                    last.then_inc(probs_done[0], 1)
                if live(i):
                    wait(dve, v_in_psum, i + 1)
                    nc.vector.tensor_tensor(v_sb[par][:, :, :, :].rearrange("p w b c -> p (w b c)"), vf_ps[:, :],
                                            neg_bv[:, :, :].rearrange("p n c -> p (n c)"),
                                            ALU.max).then_inc(v_done, 1)
                if live(i - 1):
                    wait(dve, exp_done[1], i)
                    nc.vector.reciprocal(rsum[1][:, :], sums[1][:, :]).then_inc(rsum_done[1], 1)
                if live(i):
                    for w in range(PAIR):
                        wait(dve, s_in_psum[w], i + 1)
                        nc.vector.tensor_reduce(negmax[w][:, :], s_ps[w][:, :].rearrange("p (a g) -> p a g", g=H),
                                                AX.X, ALU.max, negate=True).then_inc(max_done[w], 1)
                if live(i - 2):
                    wait(dve, o_hi_done, i - 1)
                    nc.vector.scalar_tensor_tensor(o_lo[:, :], o_ps[:, :], b_raw[:, 2:3], o_hi[:, :],
                                                   ALU.add, ALU.subtract).then_inc(o_lo_done, 1)
                if live(i + LEAD):
                    ahead = static and p + LEAD >= PAIRS
                    col = (p + LEAD - PAIRS if ahead else p + LEAD) * PAIR
                    wait(dve, x_lo_done, i + 2)
                    nc.vector.tensor_scalar(xn[nxt][:, :].rearrange("c (w h) -> c h w", h=H),
                                            Xhw[1 - buf if ahead else buf][:, :, bass.ds(col, PAIR)],
                                            mean_g[:, :], rstd_g[:, :], ALU.subtract, ALU.mult).then_inc(xn_done, 1)
                if live(i + 1):
                    wait(dve, k32_done, i + 2)
                    nc.vector.tensor_copy(k_hi[:, :], k32[:, :]).then_inc(k_hi_done, 1)
                if live(i - 1):
                    wait(dve, t_in_psum[1], i)
                    nc.vector.tensor_copy(probsT[1][:, :, :], t_ps[1][:, :].rearrange("p (b h) -> p b h", h=H)
                                          ).then_inc(probsT_done[1], 1)
                if live(i - 3):
                    behind = static and p < 3
                    col = (p - 3 + PAIRS if behind else p - 3) * PAIR
                    place = Xhw[1 - buf if behind else buf][:, :, bass.ds(col, PAIR)]
                    if not live(i - 1):
                        wait(dve, y_done, i - 2)
                    nc.vector.tensor_tensor(place, place, y[nxt][:, :].rearrange("c (w h) -> c h w", h=H),
                                            ALU.add).then_inc(res_done, 1)
                if measured:
                    chunk, loads, numbers, last_of_sample = measured
                    dve.wait_ge(loaded[1 - buf][chunk], loads * 16)
                    for n in numbers:
                        last = measure(1 - buf, n)
                    if last_of_sample:
                        last.then_inc(pieces_done, 1)

            def sample(s, buf, loads):
                base = s * PAIRS
                for p in range(0, 3):
                    step(base + p, p % 2, buf, p)
                plain, one, two, rest = range(3, 5), range(5, 13), range(13, 25), range(25, 29)
                if loads is None:
                    with dve.Fori(3, 28, 2) as p:
                        step(base + p, 1, buf, p)
                        step(base + p + 1, 0, buf, p + 1)
                else:
                    for p in plain:
                        step(base + p, p % 2, buf, p)
                    slow = len(one) // PER_CHUNK
                    for chunk in range(slow):
                        p0 = one[0] + chunk * PER_CHUNK
                        with dve.Fori(p0, p0 + PER_CHUNK - 1, 2) as p:
                            step(base + p, 1, buf, p, (chunk, loads, [p - one[0]], False))
                            step(base + p + 1, 0, buf, p + 1, (chunk, loads, [p + 1 - one[0]], False))
                    for p in two:
                        k = slow * PER_CHUNK + 2 * (p - two[0])
                        step(base + p, p % 2, buf, p, (k // PER_CHUNK, loads, [k, k + 1], k + 2 == PIECES))
                    for p, part in zip(rest, statistics):
                        step(base + p, p % 2, buf, p)
                        part(s + 1)
                for p in range(29, 32):
                    if loads is None:
                        step(N - PAIRS + p, p % 2, buf, p)
                    else:
                        if p == PAIRS - LEAD:
                            dve.wait_ge(rstd_done, s + 2)
                        step(base + p, p % 2, buf, p)

            nc.vector.memset(minus_one[:, :], -1.0)
            nc.vector.memset(minus_half[:, :], -0.5).then_inc(setup_vec, 1)
            dve.wait_ge(params_in, 9 * 16)
            dve.wait_ge(setup_vec, 1)
            nc.vector.tensor_scalar(bq_scaled[:, :], b_raw[:, 0:1], SCALE, None, ALU.mult).then_inc(setup_vec, 1)
            dve.wait_ge(wT_in_psum, 2)
            nc.vector.tensor_copy(wT_hi[:, :, :].rearrange("p n c -> p (n c)"), q_ps[:, :]).then_inc(wT_split, 1)
            nc.vector.tensor_copy(neg_bv[:, 0, :], k_ps[:, 0:C]).then_inc(wT_split, 1)
            dve.wait_ge(wT_split, 2)
            nc.vector.tensor_tensor(wT_lo[:, :, :].rearrange("p n c -> p (n c)"), q_ps[:, :],
                                    wT_hi[:, :, :].rearrange("p n c -> p (n c)"), ALU.subtract).then_inc(wT_split, 1)
            for n in range(1, PAIR * HALVES):
                last = nc.vector.tensor_copy(neg_bv[:, n, :], neg_bv[:, 0, :])
            last.then_inc(wT_split, 1)
            for chunk in range(CHUNKS):
                dve.wait_ge(loaded[0][chunk], 16)
                for n in range(chunk * PER_CHUNK, (chunk + 1) * PER_CHUNK):
                    last = measure(0, n)
            last.then_inc(pieces_done, 1)
            for part in statistics:
                part(0)
            dve.wait_ge(rstd_done, 1)
            for i in range(-LEAD, 0):
                step(i, i % 2, 0, i)

            sample(0, 0, 1)
            with dve.Fori(1, B // 2) as r:
                sample(2 * r - 1, 1, r + 1)
                sample(2 * r, 0, r + 1)
            sample(B - 1, 1, None)
            for i in range(N, N + 3):
                step(i, i % 2, 0, i - N)


_INS = ["x", "L0_conv_wq", "L0_conv_bq", "L0_conv_wk", "L0_conv_bk", "L0_conv_wv", "L0_conv_bv",
        "L0_conv_wfc", "L0_conv_bfc"]


def kernel(**inputs):
    import numpy as np
    import concourse.bacc as bacc
    from concourse.bass_utils import run_bass_kernel_spmd

    nc = bacc.Bacc("TRN2", target_bir_lowering=False, num_devices=1)
    arrays, args = {}, []
    for name in _INS:
        a = np.ascontiguousarray(inputs[name])
        arrays[f"in_{name}"] = a
        args.append(nc.dram_tensor(f"in_{name}", a.shape, mybir.dt.from_np(a.dtype), kind="ExternalInput").ap())
    shape = inputs["x"].shape
    out = nc.dram_tensor("out_x", shape, F32, kind="ExternalOutput").ap()
    build(nc, *args, out)
    r = run_bass_kernel_spmd(nc, [arrays], core_ids=[0])
    return r.results[0]["out_x"]
```

```python
from contextlib import ExitStack

import concourse.bass as bass
from concourse import mybir

F32 = mybir.dt.float32
F16 = mybir.dt.float16
ALU = mybir.AluOpType
ACT = mybir.ActivationFunctionType
AX = mybir.AxisListType

PAIR = 2
CHUNKS = 8
LEAD = 3
GROUPS = 32
EPS = 1e-5


def build(nc, x, wq, bq, wk, bk, wv, bv, wfc, bfc, out):
    B, C, H, W = x.shape
    PAIRS = W // PAIR
    N = B * PAIRS
    HW = H * W
    COLS = PAIR * H
    HALVES = H // 128
    GC = C // GROUPS
    CHUNK = HW // CHUNKS
    PIECE = 512
    PIECES = HW // PIECE
    PER_CHUNK = CHUNK // PIECE
    SCALE = float(C) ** -0.5
    assert C == 128 and H == 256 and COLS == 512 and B % 2 == 0 and PAIRS == 32

    x_dram = x.rearrange("b c h w -> b c (h w)")
    out_dram = out.rearrange("b c h w -> b c (h w)")

    with ExitStack() as ctx:
        def sb(name, shape, dt=F32):
            return ctx.enter_context(nc.sbuf_tensor(name, shape, dt))

        def bank(name):
            return ctx.enter_context(nc.psum_tensor(name, [128, 512], F32))

        def sem(name):
            return ctx.enter_context(nc.semaphore(name))

        X = [sb(f"x_sample{n}", [C, HW]) for n in range(2)]
        Xhw = [t[:, :].rearrange("c (h w) -> c h w", w=W) for t in X]
        xn = [sb(f"xn{n}", [C, H, PAIR]) for n in range(2)]
        x_hi = [sb(f"x_hi{n}", [C, H, PAIR], F16) for n in range(2)]
        x_lo = [sb(f"x_lo{n}", [C, H, PAIR], F16) for n in range(2)]
        q32, k32 = sb("q32", [C, H, PAIR]), sb("k32", [C, H, PAIR])
        q_hi, q_lo = sb("q_hi", [C, H, PAIR], F16), sb("q_lo", [C, H, PAIR], F16)
        k_hi, k_lo = sb("k_hi", [C, H, PAIR], F16), sb("k_lo", [C, H, PAIR], F16)
        v_sb = [sb(f"v{n}", [128, PAIR, HALVES, C]) for n in range(2)]
        probs = [[sb(f"probs{n}_w{w}", [128, HALVES, H]) for w in range(PAIR)] for n in range(2)]
        probsT = [sb(f"probsT_w{w}", [128, HALVES, H]) for w in range(PAIR)]
        negmax = [sb(f"negmax_w{w}", [128, HALVES]) for w in range(PAIR)]
        sums = [sb(f"sums_w{w}", [128, HALVES]) for w in range(PAIR)]
        rsum = [sb(f"rsum_w{w}", [128, HALVES]) for w in range(PAIR)]
        o_hi, o_lo = sb("o_hi", [C, H, PAIR], F16), sb("o_lo", [C, H, PAIR], F16)

        ident = sb("ident", [128, 128])
        w_raw = sb("w_raw", [128, 4, C])
        wT_hi, wT_lo = sb("wT_hi", [C, 4, C], F16), sb("wT_lo", [C, 4, C], F16)
        b_raw = sb("b_raw", [C, 4])
        bq_scaled = sb("bq_scaled", [C, 1])
        bv_row = sb("bv_row", [1, C])
        minus_one = sb("minus_one", [1, 128])
        neg_bv = sb("neg_bv", [128, PAIR * HALVES, C])

        pieces = sb("pieces", [C, PIECES, 6])
        stat = sb("stat", [C, 32])
        statT, spreadT = sb("statT", [C, 32]), sb("spreadT", [C, 32])
        groupT = sb("groupT", [C, 32 // GC])
        group = sb("group", [C, 32])
        group_sq = sb("group_sq", [C, 32])
        var_eps = sb("var_eps", [C, 1])
        minus_half = sb("minus_half", [C, 1])
        norm, norm_next = sb("norm", [C, 2]), sb("norm_next", [C, 2])

        q_ps, k_ps, vf_ps, o_ps = bank("q_ps"), bank("k_ps"), bank("vf_ps"), bank("o_ps")
        q_hw, k_hw = (t[:, :].rearrange("c (h w) -> c h w", w=PAIR) for t in (q_ps, k_ps))
        f_hw = vf_ps[:, :].rearrange("c (h w) -> c h w", w=PAIR)
        o_wh = o_ps[:, :].rearrange("c (w h) -> c w h", w=PAIR)
        s_ps = [bank(f"s_ps{w}") for w in range(PAIR)]
        t_ps = [bank(f"t_ps{w}") for w in range(PAIR)]

        params_in = sem("params_in")
        loaded = [[sem(f"loaded{n}_{c}") for c in range(CHUNKS)] for n in range(2)]
        stored = [sem(f"stored{c}") for c in range(CHUNKS)]
        ident_done, wT_in_psum, wT_split = sem("ident_done"), sem("wT_in_psum"), sem("wT_split")
        ones_done, bq_done = sem("ones_done"), sem("bq_done")
        xn_done, x_hi_done, x_lo_done = sem("xn_done"), sem("x_hi_done"), sem("x_lo_done")
        q_in_psum, k_in_psum, v_in_psum = sem("q_in_psum"), sem("k_in_psum"), sem("v_in_psum")
        q32_done, k32_done, v_done = sem("q32_done"), sem("k32_done"), sem("v_done")
        q_hi_done, q_lo_done, k_hi_done, k_lo_done = sem("q_hi_done"), sem("q_lo_done"), sem("k_hi_done"), sem("k_lo_done")
        s_in_psum = [sem(f"s_in_psum_w{w}") for w in range(PAIR)]
        max_done = [sem(f"max_done_w{w}") for w in range(PAIR)]
        exp_done = [sem(f"exp_done_w{w}") for w in range(PAIR)]
        rsum_done = [sem(f"rsum_done_w{w}") for w in range(PAIR)]
        probs_done = [sem(f"probs_done_w{w}") for w in range(PAIR)]
        t_in_psum = [sem(f"t_in_psum_w{w}") for w in range(PAIR)]
        probsT_done = [sem(f"probsT_done_w{w}") for w in range(PAIR)]
        o_in_psum, o_hi_done, o_lo_done = sem("o_in_psum"), sem("o_hi_done"), sem("o_lo_done")
        f_in_psum, y_done, res_done = sem("f_in_psum"), sem("y_done"), sem("res_done")
        pieces_done = sem("pieces_done")
        stat_chain, var_done, rstd_done = sem("stat_chain"), sem("var_done"), sem("rstd_done")

        def live(j):
            return not isinstance(j, int) or 0 <= j < N

        def wait(eng, semaphore, value):
            if not isinstance(value, int) or value > 0:
                eng.wait_ge(semaphore, value)

        def steps(eng, step, first, last):
            lo, hi = max(first, LEAD), min(last, N - LEAD - 1)
            hi -= (hi - lo + 1) % 2
            for i in range(first, lo):
                step(i, i % 2)
            with_loop = hi >= lo
            if with_loop:
                with eng.Fori(lo, hi, 2) as i:
                    step(i, lo % 2)
                    step(i + 1, (lo + 1) % 2)
            for i in range(hi + 1 if with_loop else lo, last + 1):
                step(i, i % 2)

        block = ctx.enter_context(nc.Block())

        @block.sync
        def _(sp):
            for c in range(CHUNKS):
                sp.dma_start(X[0][:, c * CHUNK:(c + 1) * CHUNK],
                             x_dram[0, :, c * CHUNK:(c + 1) * CHUNK]).then_inc(loaded[0][c], 16)
                if c == 0:
                    for n, w_dram in enumerate((wq, wk, wv, wfc)):
                        sp.dma_start(w_raw[:, n, :], w_dram).then_inc(params_in, 16)
                    for n, b_dram in enumerate((bq, bk, bv, bfc)):
                        sp.dma_start(b_raw[:, n:n + 1], b_dram.rearrange("(c a) -> c a", a=1)).then_inc(params_in, 16)
                    sp.dma_start(bv_row[:, :], bv.rearrange("(a c) -> a c", a=1)).then_inc(params_in, 16)
            for c in range(CHUNKS):
                sp.dma_start(X[1][:, c * CHUNK:(c + 1) * CHUNK],
                             x_dram[1, :, c * CHUNK:(c + 1) * CHUNK]).then_inc(loaded[1][c], 16)

            def store(s, buf, c):
                sp.dma_start(out_dram[s, :, c * CHUNK:(c + 1) * CHUNK],
                             X[buf][:, c * CHUNK:(c + 1) * CHUNK]).then_inc(stored[c], 16)

            def load(s, buf, c):
                sp.wait_ge(stored[c], (s - 1) * 16)
                sp.dma_start(X[buf][:, c * CHUNK:(c + 1) * CHUNK],
                             x_dram[s, :, c * CHUNK:(c + 1) * CHUNK]).then_inc(loaded[buf][c], 16)

            with sp.Fori(0, B - 3, 2) as s0:
                for buf in range(2):
                    s = s0 + buf
                    sp.wait_ge(res_done, (s + 1) * PAIRS)
                    for c in range(CHUNKS + 1):
                        if c < CHUNKS:
                            store(s, buf, c)
                        if c > 0:
                            load(s + 2, buf, c - 1)
            for s in (B - 2, B - 1):
                sp.wait_ge(res_done, (s + 1) * PAIRS)
                for c in range(CHUNKS):
                    store(s, s % 2, c)
            for c in range(CHUNKS):
                sp.wait_ge(stored[c], B * 16)

        @block.tensor
        def _(pe):
            def product(psum, pairs):
                for n, (stationary, moving) in enumerate(pairs):
                    last = nc.tensor.matmul(psum, stationary, moving, start=(n == 0), stop=(n == len(pairs) - 1))
                return last

            def step(i, par):
                nxt = 1 - par
                if live(i):
                    if isinstance(i, int) and i < 2:
                        wait(pe, v_done, i)
                    wait(pe, y_done, i - 2)
                    for t in range(PAIR * HALVES):
                        w, tok = t // HALVES, slice(t % HALVES * 128, (t % HALVES + 1) * 128)
                        last = product(vf_ps[:, t * C:(t + 1) * C],
                                       [(x_hi[par][:, tok, w], wT_hi[:, 2, :]), (x_hi[par][:, tok, w], wT_lo[:, 2, :]),
                                        (x_lo[par][:, tok, w], wT_hi[:, 2, :])])
                    last.then_inc(v_in_psum, 1)
                    wait(pe, k_lo_done, i + 1)
                    wait(pe, q_lo_done, i + 1)
                    for w in range(PAIR):
                        wait(pe, exp_done[w], i)
                        for a in range(HALVES):
                            rows = slice(a * 128, (a + 1) * 128)
                            last = product(s_ps[w][:, a * H:(a + 1) * H],
                                           [(q_hi[:, rows, w], k_hi[:, :, w]), (q_hi[:, rows, w], k_lo[:, :, w]),
                                            (q_lo[:, rows, w], k_hi[:, :, w])])
                        last.then_inc(s_in_psum[w], 1)
                if live(i + 1):
                    wait(pe, x_lo_done, i + 2)
                    wait(pe, res_done, i - 2)
                    for m, psum, ready in ((0, q_hw, q_in_psum), (1, k_hw, k_in_psum)):
                        product(psum, [(wT_hi[:, m, :], x_hi[nxt][:, :, :]), (wT_lo[:, m, :], x_hi[nxt][:, :, :]),
                                       (wT_hi[:, m, :], x_lo[nxt][:, :, :])]).then_inc(ready, 1)
                if live(i - 1):
                    for w in range(PAIR):
                        wait(pe, probs_done[w], i)
                        for a in range(HALVES):
                            for b in range(HALVES):
                                last = nc.tensor.transpose(t_ps[w][:, b * H + a * 128:b * H + (a + 1) * 128],
                                                           probs[nxt][w][:, a, b * 128:(b + 1) * 128], ident[:, :])
                        last.then_inc(t_in_psum[w], 1)
                if live(i - 2):
                    wait(pe, o_lo_done, i - 1)
                    wait(pe, v_done, min(i + 1, N) if isinstance(i, int) else i + 1)
                    product(f_hw, [(wT_hi[:, 3, :], o_hi[:, :, :]), (wT_lo[:, 3, :], o_hi[:, :, :]),
                                   (wT_hi[:, 3, :], o_lo[:, :, :])]).then_inc(f_in_psum, 1)
                if live(i - 1):
                    if not live(i - 2) or not live(i):
                        wait(pe, v_done, i)
                    for w in range(PAIR):
                        wait(pe, probsT_done[w], i)
                        last = product(o_ps[:, w * H:(w + 1) * H],
                                       [(v_sb[nxt][:, w, b, :], probsT[w][:, b, :]) for b in range(HALVES)])
                    last.then_inc(o_in_psum, 1)

            pe.wait_ge(ident_done, 2)
            pe.wait_ge(params_in, 9 * 16)
            for n in range(4):
                last = nc.tensor.transpose(q_ps[:, n * C:(n + 1) * C], w_raw[:, n, :], ident[:, :])
            last.then_inc(wT_in_psum, 1)
            pe.wait_ge(ones_done, 1)
            nc.tensor.matmul(k_ps[:, 0:C], minus_one[:, :], bv_row[:, :], start=True, stop=True).then_inc(wT_in_psum, 1)
            pe.wait_ge(wT_split, 4)
            steps(pe, step, -1, N + 1)

        @block.scalar
        def _(act):
            def softmax_exp(j, par, w):
                wait(act, max_done[w], j + 1)
                for a in range(HALVES):
                    last = nc.scalar.activation(probs[par][w][:, a, :], s_ps[w][:, a * H:(a + 1) * H], ACT.Exp,
                                                bias=negmax[w][:, a:a + 1], accum_out=sums[w][:, a:a + 1])
                last.then_inc(exp_done[w], 1)

            def step(i, par):
                nxt = 1 - par
                if live(i - 1):
                    softmax_exp(i - 1, nxt, 1)
                if live(i + 2):
                    wait(act, xn_done, i + 3)
                    wait(act, v_in_psum, i + 1)
                    nc.scalar.activation(x_hi[par][:, :, :], xn[par][:, :, :], ACT.Copy).then_inc(x_hi_done, 1)
                if live(i - 2):
                    wait(act, v_in_psum if live(i) else o_in_psum, i + 1 if live(i) else i - 1)
                    nc.scalar.activation(o_hi[:, :, :].rearrange("c h w -> c w h"), o_wh, ACT.Identity,
                                         bias=b_raw[:, 2:3]).then_inc(o_hi_done, 1)
                if live(i + 1):
                    wait(act, q_in_psum, i + 2)
                    nc.scalar.activation(q32[:, :, :], q_hw, ACT.Relu, bias=bq_scaled[:, :],
                                         scale=SCALE).then_inc(q32_done, 1)
                    wait(act, k_in_psum, i + 2)
                    nc.scalar.activation(k32[:, :, :], k_hw, ACT.Relu, bias=b_raw[:, 1:2]).then_inc(k32_done, 1)
                if live(i - 1):
                    wait(act, t_in_psum[0], i)
                    nc.scalar.activation(probsT[0][:, :, :], t_ps[0][:, :].rearrange("p (b h) -> p b h", h=H),
                                         ACT.Copy).then_inc(probsT_done[0], 1)
                if live(i + 1):
                    wait(act, q32_done, i + 2)
                    nc.scalar.activation(q_hi[:, :, :], q32[:, :, :], ACT.Copy).then_inc(q_hi_done, 1)
                if live(i - 2):
                    wait(act, f_in_psum, i - 1)
                    nc.scalar.activation(q_hw, f_hw, ACT.Relu, bias=b_raw[:, 3:4]).then_inc(y_done, 1)
                if live(i):
                    softmax_exp(i, par, 0)

            act.wait_ge(params_in, 9 * 16)
            nc.scalar.activation(bq_scaled[:, :], b_raw[:, 0:1], ACT.Copy, scale=SCALE).then_inc(bq_done, 1)
            act.wait_ge(bq_done, 1)
            steps(act, step, -2, N + 1)

        @block.gpsimd
        def _(pool):
            def rstd(s):
                pool.wait_ge(var_done, s + 1)
                nc.gpsimd.tensor_tensor(norm_next[:, 1:2], var_eps[:, :], minus_half[:, :], ALU.pow).then_inc(rstd_done, 1)

            def step(i, par):
                nxt = 1 - par
                if live(i - 1):
                    wait(pool, rsum_done[1], i)
                    nc.gpsimd.tensor_tensor(
                        probs[nxt][1][:, :, :], probs[nxt][1][:, :, :],
                        rsum[1][:, :].rearrange("p (a o) -> p a o", o=1).to_broadcast([128, HALVES, H]),
                        ALU.mult).then_inc(probs_done[1], 1)
                if live(i + 2):
                    wait(pool, x_hi_done, i + 3)
                    nc.gpsimd.tensor_tensor(x_lo[par][:, :, :], xn[par][:, :, :], x_hi[par][:, :, :],
                                            ALU.subtract).then_inc(x_lo_done, 1)
                if live(i + 1):
                    wait(pool, k_hi_done, i + 2)
                    nc.gpsimd.tensor_tensor(k_lo[:, :, :], k32[:, :, :], k_hi[:, :, :], ALU.subtract).then_inc(k_lo_done, 1)
                    wait(pool, q_hi_done, i + 2)
                    nc.gpsimd.tensor_tensor(q_lo[:, :, :], q32[:, :, :], q_hi[:, :, :], ALU.subtract).then_inc(q_lo_done, 1)

            nc.gpsimd.memset(ident[:, :], 0.0).then_inc(ident_done, 1)
            pool.wait_ge(ident_done, 1)
            nc.gpsimd.affine_select(out=ident[:, :], in_=ident[:, :], compare_op=ALU.not_equal, fill=1.0, base=0,
                                    pattern=[[-1, 128]], channel_multiplier=1).then_inc(ident_done, 1)
            pool.wait_ge(ones_done, 1)
            rstd(0)
            steps(pool, step, -2, PAIRS - LEAD - 2)
            with pool.Fori(1, B) as s:
                rstd(s)
                with pool.Fori(0, PAIRS - 1, 2) as p:
                    step(s * PAIRS + p - LEAD - 1, 0)
                    step(s * PAIRS + p - LEAD, 1)
            for i in range(N - LEAD - 1, N + 1):
                step(i, i % 2)

        @block.vector
        def _(dve):
            def measure(buf, n):
                return nc.vector.bn_stats(pieces[:, n, :], X[buf][:, bass.ds(n * PIECE, PIECE)])

            def chained(s, n, instruction):
                instruction.then_inc(stat_chain, 1)
                dve.wait_ge(stat_chain, s * CHAIN + n)

            CHAIN = 13

            def spread(s, n, source, result):
                chained(s, n, nc.vector.transpose(statT[:, :], source))
                chained(s, n + 1, nc.vector.tensor_reduce(groupT[:, :], statT[:, :].rearrange("p (g c) -> p g c", c=GC),
                                                          AX.X, ALU.add))
                chained(s, n + 2, nc.vector.tensor_scalar(
                    spreadT[:, :].rearrange("p (g c) -> p g c", c=GC),
                    groupT[:, :].rearrange("p (g a) -> p g a", a=1).to_broadcast([C, 32 // GC, GC]),
                    1.0 / GC, None, ALU.mult))
                chained(s, n + 3, nc.vector.transpose(result, spreadT[:, :]))

            def aggregate(s):
                dve.wait_ge(pieces_done, s + 1)
                nc.vector.memset(stat[:, 2:32], 0.0)
                chained(s, 1, nc.vector.bn_aggr(stat[:, 0:2], pieces[:, :, :].rearrange("p n k -> p (n k)")))

            def group_means(s):
                spread(s, 2, stat[:, :], group[:, :])
                chained(s, 6, nc.vector.tensor_copy(norm_next[:, 0:1], group[:, 0:1]))
                chained(s, 7, nc.vector.tensor_tensor(stat[:, 2:3], stat[:, 0:1], group[:, 0:1], ALU.subtract))
                chained(s, 8, nc.vector.tensor_tensor(stat[:, 3:4], stat[:, 2:3], stat[:, 2:3], ALU.mult))

            def group_variance(s):
                spread(s, 9, stat[:, :], group_sq[:, :])
                nc.vector.tensor_scalar(var_eps[:, :], group[:, 1:2], group_sq[:, 3:4], EPS,
                                        ALU.add, ALU.add).then_inc(var_done, 1)

            def hand_over(s):
                wait(dve, xn_done, s * PAIRS)
                dve.wait_ge(rstd_done, s + 1)
                chained(s, 13, nc.vector.tensor_copy(norm[:, :], norm_next[:, :]))

            statistics = (aggregate, group_means, group_variance, hand_over)

            def step(i, par, buf, p, measured=None, statistic=None):
                nxt = 1 - par
                static = isinstance(p, int)
                if live(i - 1):
                    wait(dve, exp_done[0], i)
                    nc.vector.reciprocal(rsum[0][:, :], sums[0][:, :]).then_inc(rsum_done[0], 1)
                    wait(dve, rsum_done[0], i)
                    for a in range(HALVES):
                        last = nc.vector.tensor_scalar(probs[nxt][0][:, a, :], probs[nxt][0][:, a, :],
                                                       rsum[0][:, a:a + 1], None, ALU.mult)
                    last.then_inc(probs_done[0], 1)
                if live(i):
                    wait(dve, v_in_psum, i + 1)
                    nc.vector.tensor_tensor(v_sb[par][:, :, :, :].rearrange("p w b c -> p (w b c)"), vf_ps[:, :],
                                            neg_bv[:, :, :].rearrange("p n c -> p (n c)"),
                                            ALU.max).then_inc(v_done, 1)
                if live(i - 1):
                    wait(dve, exp_done[1], i)
                    nc.vector.reciprocal(rsum[1][:, :], sums[1][:, :]).then_inc(rsum_done[1], 1)
                if live(i):
                    for w in range(PAIR):
                        wait(dve, s_in_psum[w], i + 1)
                        nc.vector.tensor_reduce(negmax[w][:, :], s_ps[w][:, :].rearrange("p (a g) -> p a g", g=H),
                                                AX.X, ALU.max, negate=True).then_inc(max_done[w], 1)
                if live(i - 2):
                    wait(dve, o_hi_done, i - 1)
                    nc.vector.scalar_tensor_tensor(o_lo[:, :, :].rearrange("c h w -> c w h"), o_wh, b_raw[:, 2:3],
                                                   o_hi[:, :, :].rearrange("c h w -> c w h"),
                                                   ALU.add, ALU.subtract).then_inc(o_lo_done, 1)
                if live(i + LEAD):
                    ahead = static and p + LEAD >= PAIRS
                    col = (p + LEAD - PAIRS if ahead else p + LEAD) * PAIR
                    wait(dve, x_lo_done, i + 2)
                    nc.vector.tensor_scalar(xn[nxt][:, :, :],
                                            Xhw[1 - buf if ahead else buf][:, :, bass.ds(col, PAIR)],
                                            norm[:, 0:1], norm[:, 1:2], ALU.subtract, ALU.mult).then_inc(xn_done, 1)
                if live(i + 1):
                    wait(dve, k32_done, i + 2)
                    nc.vector.tensor_copy(k_hi[:, :, :], k32[:, :, :]).then_inc(k_hi_done, 1)
                if live(i - 1):
                    wait(dve, t_in_psum[1], i)
                    nc.vector.tensor_copy(probsT[1][:, :, :], t_ps[1][:, :].rearrange("p (b h) -> p b h", h=H)
                                          ).then_inc(probsT_done[1], 1)
                if measured:
                    chunk, loads, numbers, last_of_sample = measured
                    dve.wait_ge(loaded[1 - buf][chunk], loads * 16)
                    for n in numbers:
                        last = measure(1 - buf, n)
                    if last_of_sample:
                        last.then_inc(pieces_done, 1)
                if statistic:
                    part, s = statistic
                    part(s)
                if live(i - 2):
                    behind = static and p < 2
                    col = (p - 2 + PAIRS if behind else p - 2) * PAIR
                    place = Xhw[1 - buf if behind else buf][:, :, bass.ds(col, PAIR)]
                    wait(dve, y_done, i - 1)
                    nc.vector.tensor_tensor(place, place, q_hw, ALU.add).then_inc(res_done, 1)

            def sample(s, buf, loads):
                base = s * PAIRS
                for p in range(0, 3):
                    step(base + p, p % 2, buf, p)
                plain, one, two, rest = range(3, 5), range(5, 13), range(13, 25), range(25, 29)
                if loads is None:
                    with dve.Fori(3, 28, 2) as p:
                        step(base + p, 1, buf, p)
                        step(base + p + 1, 0, buf, p + 1)
                else:
                    for p in plain:
                        step(base + p, p % 2, buf, p)
                    slow = len(one) // PER_CHUNK
                    for chunk in range(slow):
                        p0 = one[0] + chunk * PER_CHUNK
                        with dve.Fori(p0, p0 + PER_CHUNK - 1, 2) as p:
                            step(base + p, 1, buf, p, (chunk, loads, [p - one[0]], False))
                            step(base + p + 1, 0, buf, p + 1, (chunk, loads, [p + 1 - one[0]], False))
                    for p in two:
                        k = slow * PER_CHUNK + 2 * (p - two[0])
                        step(base + p, p % 2, buf, p, (k // PER_CHUNK, loads, [k, k + 1], k + 2 == PIECES))
                    for p, part in zip(rest, statistics):
                        step(base + p, p % 2, buf, p, statistic=(part, s + 1))
                for p in range(29, 32):
                    step(base + p, p % 2, buf, p)

            nc.vector.memset(minus_one[:, :], -1.0)
            nc.vector.memset(minus_half[:, :], -0.5).then_inc(ones_done, 1)
            dve.wait_ge(params_in, 9 * 16)
            dve.wait_ge(wT_in_psum, 2)
            nc.vector.tensor_copy(wT_hi[:, :, :].rearrange("p n c -> p (n c)"), q_ps[:, :]).then_inc(wT_split, 1)
            nc.vector.tensor_copy(neg_bv[:, 0, :], k_ps[:, 0:C]).then_inc(wT_split, 1)
            dve.wait_ge(wT_split, 2)
            nc.vector.tensor_tensor(wT_lo[:, :, :].rearrange("p n c -> p (n c)"), q_ps[:, :],
                                    wT_hi[:, :, :].rearrange("p n c -> p (n c)"), ALU.subtract).then_inc(wT_split, 1)
            for n in range(1, PAIR * HALVES):
                last = nc.vector.tensor_copy(neg_bv[:, n, :], neg_bv[:, 0, :])
            last.then_inc(wT_split, 1)
            for chunk in range(CHUNKS):
                dve.wait_ge(loaded[0][chunk], 16)
                for n in range(chunk * PER_CHUNK, (chunk + 1) * PER_CHUNK):
                    last = measure(0, n)
            last.then_inc(pieces_done, 1)
            for part in statistics:
                part(0)
            for i in range(-LEAD, 0):
                step(i, i % 2, 0, i)

            sample(0, 0, 1)
            with dve.Fori(1, B // 2) as r:
                sample(2 * r - 1, 1, r + 1)
                sample(2 * r, 0, r + 1)
            sample(B - 1, 1, None)
            for i in range(N, N + 2):
                step(i, i % 2, 0, i - N)


_INS = ["x", "L0_conv_wq", "L0_conv_bq", "L0_conv_wk", "L0_conv_bk", "L0_conv_wv", "L0_conv_bv",
        "L0_conv_wfc", "L0_conv_bfc"]


def kernel(**inputs):
    import numpy as np
    import concourse.bacc as bacc
    from concourse.bass_utils import run_bass_kernel_spmd

    nc = bacc.Bacc("TRN2", target_bir_lowering=False, num_devices=1)
    arrays, args = {}, []
    for name in _INS:
        a = np.ascontiguousarray(inputs[name])
        arrays[f"in_{name}"] = a
        args.append(nc.dram_tensor(f"in_{name}", a.shape, mybir.dt.from_np(a.dtype), kind="ExternalInput").ap())
    shape = inputs["x"].shape
    out = nc.dram_tensor("out_x", shape, F32, kind="ExternalOutput").ap()
    build(nc, *args, out)
    r = run_bass_kernel_spmd(nc, [arrays], core_ids=[0])
    return r.results[0]["out_x"]
```
